# Optimizing a Trainium2 kernel written in Bass

```python
import numpy as np
import jax
import jax.numpy as jnp

def _softmax(x, axis=-1):
    return jax.nn.softmax(x, axis=axis)

def _gelu(x):
    return jax.nn.gelu(x, approximate=True)

def _silu(x):
    return jax.nn.silu(x)

def _sigmoid(x):
    return jax.nn.sigmoid(x)

def _layernorm(x, axis=-1, eps=1e-05):
    m = jnp.mean(x, axis=axis, keepdims=True)
    v = jnp.var(x, axis=axis, keepdims=True)
    return (x - m) / jnp.sqrt(v + eps)

def _scatter_add(tgt, idx, src, axis=0):
    return tgt.at[idx].add(src)

def _segment_sum(src, seg, n):
    return jax.ops.segment_sum(src, seg, n)
kernel_name = 'mk_rec_standalone_d1_rec_r8_c3920b'

def setup_inputs(seed: int=0):
    np.random.seed(seed)
    _w = jnp.asarray

    def _rec_inputs():
        import jax
        import jax.numpy as jnp
        _rk = jax.random.key(seed)
        r_x0 = jax.random.randint(jax.random.fold_in(_rk, 1), (1024, 12500), 0, 2, jnp.int32)
        return r_x0
    r_x0 = _rec_inputs()

    def _L0_rec_setup():
        import jax, jax.numpy as jnp
        import numpy as np
        FIELD_DIMS = 12500
        FACTORS = 16
        BATCH = 1024
        key = jax.random.key(seed)
        k1, k2 = jax.random.split(key)
        x0 = jax.random.randint(k1, (BATCH, FIELD_DIMS), 0, 2, dtype=jnp.int32)
        W = jax.random.normal(k2, (FIELD_DIMS, FACTORS), dtype=jnp.float32) * 0.05
        return {'x0': x0, 'W': W}
    _L0_rec_all = _L0_rec_setup()
    _L0_rec_in = {k: v for k, v in _L0_rec_all.items() if k in ('W',)}
    del _L0_rec_all
    return {'r_x0': r_x0, 'L0_rec_W': _L0_rec_in['W']}

def reference(r_x0, L0_rec_W):
    import jax
    import jax.numpy as jnp

    def _L0_rec_ref(x0, W):
        import jax, jax.numpy as jnp
        import numpy as np
        FIELD_DIMS = 12500
        FACTORS = 16
        BATCH = 1024
        m = (x0 > 0).astype(W.dtype)
        s = m @ W
        q = m @ jnp.sum(W * W, axis=-1)
        return 0.5 * (jnp.sum(s * s, axis=-1) - q)
    y = _L0_rec_ref(r_x0, L0_rec_W)
    return y

_drawn_inputs = setup_inputs


def setup_inputs(seed=0):
    import zlib

    import numpy as np

    out = dict(_drawn_inputs(seed))
    spreads = {}
    factors = {}
    for name, (base, spread) in spreads.items():
        noise = np.random.default_rng([zlib.crc32(name.encode()), seed]).standard_normal(out[name].shape)
        drawn = base * np.exp(spread * noise) if base else spread * noise
        out[name] = jnp.asarray(drawn.astype(out[name].dtype))
    for name, factor in factors.items():
        out[name] = (out[name] * factor).astype(out[name].dtype)
    return out
```

```python
from contextlib import ExitStack

import concourse.bass as bass
from concourse import mybir

ALU = mybir.AluOpType
AX_X = mybir.AxisListType.X
F32 = mybir.dt.float32
BF16 = mybir.dt.bfloat16
I32 = mybir.dt.int32

P = 128
GROUP = 4
SLOTS = 4
ROUND = GROUP * SLOTS
PARTS = 3


def build(nc: bass.Bass, xT: bass.AP, W: bass.AP, out: bass.AP):
    FIELDS, BATCH = xT.shape
    FACTORS = W.shape[1]
    COLS = FACTORS + 1
    TILES = BATCH // P
    CHUNKS = FIELDS // P
    REST = FIELDS - CHUNKS * P
    WHOLE = CHUNKS * P
    ROUNDS = CHUNKS // ROUND
    LAST_ROUND = (ROUNDS - 1) * ROUND
    assert CHUNKS == ROUNDS * ROUND + 1 and ROUNDS >= 3 and 0 < REST < P and BATCH % P == 0

    x_rows = xT[0:WHOLE, :].rearrange("(p c) b -> p c b", c=CHUNKS)
    w_rows = W[0:WHOLE, :].rearrange("(p c) f -> p c f", c=CHUNKS)

    PIECES = [(0, 2), (2, 1), (3, 1)]

    with ExitStack() as ctx:
        def sb(name, shape, dt):
            return ctx.enter_context(nc.sbuf_tensor(name, shape, dt))

        def sem(name):
            return ctx.enter_context(nc.semaphore(name))

        x_ring = sb("x_ring", [P, SLOTS, GROUP, BATCH], I32)
        x_edge = sb("x_edge", [P, BATCH], I32)
        masks = sb("masks", [P, SLOTS, GROUP, BATCH], BF16)
        mask_rest = sb("mask_rest", [P, BATCH], BF16)
        w = sb("w", [P, CHUNKS + 1, FACTORS], F32)
        w_left = sb("w_left", [P, CHUNKS + 1, FACTORS], F32)
        w_sq = sb("w_sq", [P, CHUNKS + 1, FACTORS], F32)
        q = sb("q", [P, CHUNKS + 1], F32)
        q_half = sb("q_half", [P, CHUNKS + 1], F32)
        q_left = sb("q_left", [P, CHUNKS + 1], F32)
        wq_parts = sb("wq_parts", [P, CHUNKS + 1, PARTS, COLS], BF16)
        sums = sb("sums", [P, TILES, COLS], F32)
        sums_sq = sb("sums_sq", [P, TILES, FACTORS], F32)
        sq_total = sb("sq_total", [P, TILES], F32)
        y = sb("y", [P, TILES], F32)
        acc = ctx.enter_context(nc.psum_tensor("acc", [P, TILES, 512], F32))

        w_zeroed = sem("w_zeroed")
        w_loaded = sem("w_loaded")
        w_squared = sem("w_squared")
        x_loaded = [sem(f"x_loaded{s}") for s in range(SLOTS)]
        piece_loaded = [sem(f"piece_loaded{n}") for n in range(len(PIECES))]
        rest_loaded = sem("rest_loaded")
        last_loaded = sem("last_loaded")
        prep_done = sem("prep_done")
        mask_ready = sem("mask_ready")
        group_used = sem("group_used")
        acc_done = sem("acc_done")
        close_done = sem("close_done")
        out_stored = sem("out_stored")

        PREP_STEPS = 10
        CLOSE_STEPS = 4

        def masks_up_to(chunk):
            return chunk + 2

        block = ctx.enter_context(nc.Block())

        @block.sync
        def _(sp):
            sp.dma_start(w[:, 0:CHUNKS, :], w_rows).then_inc(w_loaded, 16)
            sp.dma_start(x_edge[0:REST, :], xT[WHOLE:FIELDS, :]).then_inc(rest_loaded, 16)
            for s in range(SLOTS):
                sp.dma_start(x_ring[:, s, :, :],
                             x_rows[:, s * GROUP:(s + 1) * GROUP, :]).then_inc(x_loaded[s], 16)

            with sp.Fori(ROUND, LAST_ROUND, ROUND) as first:
                for s in range(SLOTS):
                    sp.wait_ge(mask_ready, first + (masks_up_to((s + 1) * GROUP - 1) - ROUND))
                    sp.dma_start(x_ring[:, s, :, :],
                                 x_rows[:, bass.ds(first + s * GROUP, GROUP), :]).then_inc(x_loaded[s], 16)

            for s in range(SLOTS - 1):
                sp.wait_ge(mask_ready, masks_up_to(LAST_ROUND - ROUND + (s + 1) * GROUP - 1))
                c = LAST_ROUND + s * GROUP
                sp.dma_start(x_ring[:, s, :, :], x_rows[:, c:c + GROUP, :]).then_inc(x_loaded[s], 16)
            sp.wait_ge(mask_ready, masks_up_to(LAST_ROUND - 1))
            for n, (a, k) in enumerate(PIECES):
                c = LAST_ROUND + (SLOTS - 1) * GROUP + a
                sp.dma_start(x_ring[:, SLOTS - 1, a:a + k, :],
                             x_rows[:, c:c + k, :]).then_inc(piece_loaded[n], 16)
            sp.dma_start(x_edge[:, :], x_rows[:, CHUNKS - 1, :]).then_inc(last_loaded, 16)

            sp.wait_ge(close_done, CLOSE_STEPS)
            sp.dma_start(out, y[:, :]).then_inc(out_stored, 16)
            sp.wait_ge(out_stored, 16)

        @block.scalar
        def _(act):
            act.wait_ge(w_zeroed, 1)
            act.dma_start(w[0:REST, CHUNKS, :], W[WHOLE:FIELDS, :]).then_inc(w_loaded, 16)

        @block.gpsimd
        def _(pool):
            nc.gpsimd.memset(w[:, CHUNKS, :], 0.0).then_inc(w_zeroed, 1)
            pool.wait_ge(w_loaded, 32)
            nc.gpsimd.tensor_tensor(w_sq[:, :, :], w[:, :, :], w[:, :, :], ALU.mult).then_inc(w_squared, 1)

        @block.vector
        def _(dve):
            def w_part(t):
                return wq_parts[:, :, t, 0:FACTORS]

            def q_part(t):
                return wq_parts[:, :, t, FACTORS]

            dve.wait_ge(w_loaded, 32)
            nc.vector.tensor_copy(w_part(0), w[:, :, :]).then_inc(prep_done, 1)
            dve.wait_ge(prep_done, 1)
            nc.vector.tensor_tensor(w_left[:, :, :], w[:, :, :], w_part(0), ALU.subtract).then_inc(prep_done, 1)
            dve.wait_ge(prep_done, 2)
            nc.vector.tensor_copy(w_part(1), w_left[:, :, :]).then_inc(prep_done, 1)
            dve.wait_ge(prep_done, 3)
            nc.vector.tensor_tensor(w_part(2), w_left[:, :, :], w_part(1), ALU.subtract).then_inc(prep_done, 1)
            dve.wait_ge(w_squared, 1)
            nc.vector.tensor_reduce(q[:, :], w_sq[:, :, :], AX_X, ALU.add).then_inc(prep_done, 1)
            dve.wait_ge(prep_done, 5)
            nc.vector.tensor_scalar(q_half[:, :], q[:, :], 0.5, None, ALU.mult).then_inc(prep_done, 1)
            dve.wait_ge(prep_done, 6)
            nc.vector.tensor_copy(q_part(0), q_half[:, :]).then_inc(prep_done, 1)
            dve.wait_ge(prep_done, 7)
            nc.vector.tensor_tensor(q_left[:, :], q_half[:, :], q_part(0), ALU.subtract).then_inc(prep_done, 1)
            dve.wait_ge(prep_done, 8)
            nc.vector.tensor_copy(q_part(1), q_left[:, :]).then_inc(prep_done, 1)
            dve.wait_ge(prep_done, 9)
            nc.vector.tensor_tensor(q_part(2), q_left[:, :], q_part(1), ALU.subtract).then_inc(prep_done, 1)

            def make_mask(dst, src):
                nc.vector.tensor_scalar(dst, src, 0.0, None, ALU.is_gt).then_inc(mask_ready, 1)

            def ring_masks(s, a, k):
                for c in range(a, a + k):
                    make_mask(masks[:, s, c, :], x_ring[:, s, c, :])

            dve.wait_ge(rest_loaded, 16)
            make_mask(mask_rest[0:REST, :], x_edge[0:REST, :])
            for s in range(SLOTS):
                dve.wait_ge(x_loaded[s], 16)
                ring_masks(s, 0, GROUP)

            with dve.Fori(1, ROUNDS - 1) as turn:
                for s in range(SLOTS):
                    dve.wait_ge(x_loaded[s], (turn + 1) * 16)
                    dve.wait_ge(group_used, turn * SLOTS + (s + 1 - SLOTS))
                    ring_masks(s, 0, GROUP)

            for s in range(SLOTS - 1):
                dve.wait_ge(x_loaded[s], ROUNDS * 16)
                dve.wait_ge(group_used, (ROUNDS - 2) * SLOTS + s + 1)
                ring_masks(s, 0, GROUP)
            dve.wait_ge(group_used, (ROUNDS - 1) * SLOTS)
            for n, (a, k) in enumerate(PIECES):
                dve.wait_ge(piece_loaded[n], 16)
                ring_masks(SLOTS - 1, a, k)
            dve.wait_ge(last_loaded, 16)
            dve.wait_ge(group_used, (ROUNDS - 1) * SLOTS + 1)
            make_mask(masks[:, 0, 0, :], x_edge[:, :])

            dve.wait_ge(acc_done, 1)
            nc.vector.tensor_reduce(
                sums[:, :, :], acc[:, :, 0:PARTS * COLS].rearrange("p j (t f) -> p j f t", t=PARTS),
                AX_X, ALU.add).then_inc(close_done, 1)
            dve.wait_ge(close_done, 1)
            nc.vector.tensor_tensor(sums_sq[:, :, :], sums[:, :, 0:FACTORS], sums[:, :, 0:FACTORS],
                                    ALU.mult).then_inc(close_done, 1)
            dve.wait_ge(close_done, 2)
            nc.vector.tensor_reduce(sq_total[:, :], sums_sq[:, :, :], AX_X, ALU.add).then_inc(close_done, 1)
            dve.wait_ge(close_done, 3)
            nc.vector.scalar_tensor_tensor(out=y[:, :], in0=sq_total[:, :], scalar=0.5,
                                           in1=sums[:, :, FACTORS], op0=ALU.mult,
                                           op1=ALU.subtract).then_inc(close_done, 1)

        @block.tensor
        def _(pe):
            def products(mask, weights, start=False, stop=False):
                for j in range(TILES):
                    last = nc.tensor.matmul(acc[:, j, 0:PARTS * COLS], mask[:, j * P:(j + 1) * P], weights,
                                            start=start, stop=stop, skip_group_check=True)
                return last

            def weights_of(chunk):
                return wq_parts[:, bass.ds(chunk, 1), :, :].rearrange("p c t f -> p (c t f)")

            pe.wait_ge(prep_done, PREP_STEPS)
            pe.wait_ge(mask_ready, 1)
            products(mask_rest[0:REST, :],
                     wq_parts[0:REST, CHUNKS, :, :].rearrange("p t f -> p (t f)"), start=True)

            with pe.Fori(0, LAST_ROUND, ROUND) as first:
                for s in range(SLOTS):
                    for c in range(GROUP):
                        n = s * GROUP + c
                        pe.wait_ge(mask_ready, first + masks_up_to(n))
                        last = products(masks[:, s, c, :], weights_of(first + n))
                    last.then_inc(group_used, 1)

            for s in range(SLOTS):
                for c in range(GROUP):
                    n = LAST_ROUND + s * GROUP + c
                    pe.wait_ge(mask_ready, masks_up_to(n))
                    last = products(masks[:, s, c, :], weights_of(n))
                last.then_inc(group_used, 1)
            pe.wait_ge(mask_ready, masks_up_to(CHUNKS - 1))
            products(masks[:, 0, 0, :], weights_of(CHUNKS - 1), stop=True).then_inc(acc_done, 1)


def kernel(r_x0, L0_rec_W):
    import numpy as np
    import concourse.bacc as bacc
    from concourse.bass_utils import run_bass_kernel_spmd

    xT = np.ascontiguousarray(np.asarray(r_x0).T)
    W = np.ascontiguousarray(np.asarray(L0_rec_W))
    batch = xT.shape[1]

    nc = bacc.Bacc("TRN2", target_bir_lowering=False, num_devices=1)
    xT_dram = nc.dram_tensor("xT_dram", xT.shape, I32, kind="ExternalInput").ap()
    W_dram = nc.dram_tensor("W_dram", W.shape, F32, kind="ExternalInput").ap()
    out_dram = nc.dram_tensor("out_dram", (P, batch // P), F32, kind="ExternalOutput").ap()
    build(nc, xT_dram, W_dram, out_dram)
    r = run_bass_kernel_spmd(nc, [{"xT_dram": xT, "W_dram": W}], core_ids=[0])
    return np.ascontiguousarray(r.results[0]["out_dram"].T).reshape(batch)
```

```python
from contextlib import ExitStack

import concourse.bass as bass
from concourse import mybir

ALU = mybir.AluOpType
AX_X = mybir.AxisListType.X
F32 = mybir.dt.float32
BF16 = mybir.dt.bfloat16
I32 = mybir.dt.int32

P = 128
GROUP = 4
SLOTS = 4
ROUND = GROUP * SLOTS
PARTS = 3


def build(nc: bass.Bass, xT: bass.AP, W: bass.AP, out: bass.AP):
    FIELDS, BATCH = xT.shape
    FACTORS = W.shape[1]
    COLS = FACTORS + 1
    TILES = BATCH // P
    CHUNKS = FIELDS // P
    REST = FIELDS - CHUNKS * P
    WHOLE = CHUNKS * P
    ROUNDS = CHUNKS // ROUND
    LAST_ROUND = (ROUNDS - 1) * ROUND
    assert CHUNKS == ROUNDS * ROUND + 1 and ROUNDS >= 3 and 0 < REST < P and BATCH % P == 0

    x_rows = xT[0:WHOLE, :].rearrange("(p c) b -> p c b", c=CHUNKS)
    w_rows = W[0:WHOLE, :].rearrange("(p c) f -> p c f", c=CHUNKS)

    PIECES = [(0, 2), (2, 1), (3, 1)]
    BATCH_PARTS = [(0, TILES // 2), (TILES // 2, TILES // 4), (TILES * 3 // 4, TILES // 4)]

    with ExitStack() as ctx:
        def sb(name, shape, dt):
            return ctx.enter_context(nc.sbuf_tensor(name, shape, dt))

        def sem(name):
            return ctx.enter_context(nc.semaphore(name))

        x_ring = sb("x_ring", [P, SLOTS, GROUP, BATCH], I32)
        x_edge = sb("x_edge", [P, BATCH], I32)
        masks = sb("masks", [P, SLOTS, GROUP, BATCH], BF16)
        mask_rest = sb("mask_rest", [P, BATCH], BF16)
        w = sb("w", [P, CHUNKS + 1, FACTORS], F32)
        w_left = sb("w_left", [P, CHUNKS + 1, FACTORS], F32)
        w_sq = sb("w_sq", [P, CHUNKS + 1, FACTORS], F32)
        q = sb("q", [P, CHUNKS + 1], F32)
        q_half = sb("q_half", [P, CHUNKS + 1], F32)
        q_left = sb("q_left", [P, CHUNKS + 1], F32)
        wq_parts = sb("wq_parts", [P, CHUNKS + 1, PARTS, COLS], BF16)
        sums = sb("sums", [P, TILES, COLS], F32)
        y = sb("y", [P, TILES], F32)
        acc = ctx.enter_context(nc.psum_tensor("acc", [P, TILES, 512], F32))

        w_zeroed = sem("w_zeroed")
        w_loaded = sem("w_loaded")
        w_squared = sem("w_squared")
        x_loaded = [sem(f"x_loaded{s}") for s in range(SLOTS)]
        piece_loaded = [sem(f"piece_loaded{n}") for n in range(len(PIECES))]
        rest_loaded = sem("rest_loaded")
        last_loaded = [sem(f"last_loaded{n}") for n in range(len(BATCH_PARTS))]
        prep_done = sem("prep_done")
        mask_ready = sem("mask_ready")
        group_used = sem("group_used")
        acc_done = sem("acc_done")
        close_done = sem("close_done")
        out_stored = sem("out_stored")

        PREP_STEPS = 10
        CLOSE_STEPS = len(BATCH_PARTS) + 2

        def masks_up_to(chunk):
            return chunk + 2

        block = ctx.enter_context(nc.Block())

        @block.sync
        def _(sp):
            sp.dma_start(w[:, 0:CHUNKS, :], w_rows).then_inc(w_loaded, 16)
            sp.dma_start(x_edge[0:REST, :], xT[WHOLE:FIELDS, :]).then_inc(rest_loaded, 16)
            for s in range(SLOTS):
                sp.dma_start(x_ring[:, s, :, :],
                             x_rows[:, s * GROUP:(s + 1) * GROUP, :]).then_inc(x_loaded[s], 16)

            with sp.Fori(ROUND, LAST_ROUND, ROUND) as first:
                for s in range(SLOTS):
                    sp.wait_ge(mask_ready, first + (masks_up_to((s + 1) * GROUP - 1) - ROUND))
                    sp.dma_start(x_ring[:, s, :, :],
                                 x_rows[:, bass.ds(first + s * GROUP, GROUP), :]).then_inc(x_loaded[s], 16)

            for s in range(SLOTS - 1):
                sp.wait_ge(mask_ready, masks_up_to(LAST_ROUND - ROUND + (s + 1) * GROUP - 1))
                c = LAST_ROUND + s * GROUP
                sp.dma_start(x_ring[:, s, :, :], x_rows[:, c:c + GROUP, :]).then_inc(x_loaded[s], 16)
            sp.wait_ge(mask_ready, masks_up_to(LAST_ROUND - 1))
            for n, (a, k) in enumerate(PIECES):
                c = LAST_ROUND + (SLOTS - 1) * GROUP + a
                sp.dma_start(x_ring[:, SLOTS - 1, a:a + k, :],
                             x_rows[:, c:c + k, :]).then_inc(piece_loaded[n], 16)
            for n, (j, k) in enumerate(BATCH_PARTS):
                sp.dma_start(x_edge[:, j * P:(j + k) * P],
                             x_rows[:, CHUNKS - 1, j * P:(j + k) * P]).then_inc(last_loaded[n], 16)

            sp.wait_ge(close_done, CLOSE_STEPS)
            sp.dma_start(out, y[:, :]).then_inc(out_stored, 16)
            sp.wait_ge(out_stored, 16)

        @block.scalar
        def _(act):
            act.wait_ge(w_zeroed, 1)
            act.dma_start(w[0:REST, CHUNKS, :], W[WHOLE:FIELDS, :]).then_inc(w_loaded, 16)

        @block.gpsimd
        def _(pool):
            nc.gpsimd.memset(w[:, CHUNKS, :], 0.0).then_inc(w_zeroed, 1)
            pool.wait_ge(w_loaded, 32)
            nc.gpsimd.tensor_tensor(w_sq[:, :, :], w[:, :, :], w[:, :, :], ALU.mult).then_inc(w_squared, 1)

        @block.vector
        def _(dve):
            def w_part(t):
                return wq_parts[:, :, t, 0:FACTORS]

            def q_part(t):
                return wq_parts[:, :, t, FACTORS]

            dve.wait_ge(w_loaded, 32)
            nc.vector.tensor_copy(w_part(0), w[:, :, :]).then_inc(prep_done, 1)
            dve.wait_ge(prep_done, 1)
            nc.vector.tensor_tensor(w_left[:, :, :], w[:, :, :], w_part(0), ALU.subtract).then_inc(prep_done, 1)
            dve.wait_ge(prep_done, 2)
            nc.vector.tensor_copy(w_part(1), w_left[:, :, :]).then_inc(prep_done, 1)
            dve.wait_ge(prep_done, 3)
            nc.vector.tensor_tensor(w_part(2), w_left[:, :, :], w_part(1), ALU.subtract).then_inc(prep_done, 1)
            dve.wait_ge(w_squared, 1)
            nc.vector.tensor_reduce(q[:, :], w_sq[:, :, :], AX_X, ALU.add).then_inc(prep_done, 1)
            dve.wait_ge(prep_done, 5)
            nc.vector.tensor_scalar(q_half[:, :], q[:, :], -0.5, None, ALU.mult).then_inc(prep_done, 1)
            dve.wait_ge(prep_done, 6)
            nc.vector.tensor_copy(q_part(0), q_half[:, :]).then_inc(prep_done, 1)
            dve.wait_ge(prep_done, 7)
            nc.vector.tensor_tensor(q_left[:, :], q_half[:, :], q_part(0), ALU.subtract).then_inc(prep_done, 1)
            dve.wait_ge(prep_done, 8)
            nc.vector.tensor_copy(q_part(1), q_left[:, :]).then_inc(prep_done, 1)
            dve.wait_ge(prep_done, 9)
            nc.vector.tensor_tensor(q_part(2), q_left[:, :], q_part(1), ALU.subtract).then_inc(prep_done, 1)

            def make_mask(dst, src):
                nc.vector.tensor_scalar(dst, src, 0.0, None, ALU.is_gt).then_inc(mask_ready, 1)

            def ring_masks(s, a, k):
                for c in range(a, a + k):
                    make_mask(masks[:, s, c, :], x_ring[:, s, c, :])

            dve.wait_ge(rest_loaded, 16)
            make_mask(mask_rest[0:REST, :], x_edge[0:REST, :])
            for s in range(SLOTS):
                dve.wait_ge(x_loaded[s], 16)
                ring_masks(s, 0, GROUP)

            with dve.Fori(1, ROUNDS - 1) as turn:
                for s in range(SLOTS):
                    dve.wait_ge(x_loaded[s], (turn + 1) * 16)
                    dve.wait_ge(group_used, turn * SLOTS + (s + 1 - SLOTS))
                    ring_masks(s, 0, GROUP)

            for s in range(SLOTS - 1):
                dve.wait_ge(x_loaded[s], ROUNDS * 16)
                dve.wait_ge(group_used, (ROUNDS - 2) * SLOTS + s + 1)
                ring_masks(s, 0, GROUP)
            dve.wait_ge(group_used, (ROUNDS - 1) * SLOTS)
            for n, (a, k) in enumerate(PIECES):
                dve.wait_ge(piece_loaded[n], 16)
                ring_masks(SLOTS - 1, a, k)
            dve.wait_ge(group_used, (ROUNDS - 1) * SLOTS + 1)
            for n, (j, k) in enumerate(BATCH_PARTS):
                dve.wait_ge(last_loaded[n], 16)
                make_mask(masks[:, 0, 0, j * P:(j + k) * P], x_edge[:, j * P:(j + k) * P])

            for n, (j, k) in enumerate(BATCH_PARTS):
                dve.wait_ge(acc_done, n + 1)
                nc.vector.tensor_reduce(
                    sums[:, j:j + k, :],
                    acc[:, j:j + k, 0:PARTS * COLS].rearrange("p j (t f) -> p j f t", t=PARTS),
                    AX_X, ALU.add).then_inc(close_done, 1)
            dve.wait_ge(close_done, len(BATCH_PARTS))
            nc.vector.scalar_tensor_tensor(out=sums[:, :, 0:FACTORS], in0=sums[:, :, 0:FACTORS], scalar=0.5,
                                           in1=sums[:, :, 0:FACTORS], op0=ALU.mult,
                                           op1=ALU.mult).then_inc(close_done, 1)
            dve.wait_ge(close_done, len(BATCH_PARTS) + 1)
            nc.vector.tensor_reduce(y[:, :], sums[:, :, :], AX_X, ALU.add).then_inc(close_done, 1)

        @block.tensor
        def _(pe):
            def products(mask, weights, start=False, stop=False, tiles=range(TILES)):
                for j in tiles:
                    last = nc.tensor.matmul(acc[:, j, 0:PARTS * COLS], mask[:, j * P:(j + 1) * P], weights,
                                            start=start, stop=stop, skip_group_check=True)
                return last

            def weights_of(chunk):
                return wq_parts[:, bass.ds(chunk, 1), :, :].rearrange("p c t f -> p (c t f)")

            pe.wait_ge(prep_done, PREP_STEPS)
            pe.wait_ge(mask_ready, 1)
            products(mask_rest[0:REST, :],
                     wq_parts[0:REST, CHUNKS, :, :].rearrange("p t f -> p (t f)"), start=True)

            with pe.Fori(0, LAST_ROUND, ROUND) as first:
                for s in range(SLOTS):
                    for c in range(GROUP):
                        n = s * GROUP + c
                        pe.wait_ge(mask_ready, first + masks_up_to(n))
                        last = products(masks[:, s, c, :], weights_of(first + n))
                    last.then_inc(group_used, 1)

            for s in range(SLOTS):
                for c in range(GROUP):
                    n = LAST_ROUND + s * GROUP + c
                    pe.wait_ge(mask_ready, masks_up_to(n))
                    last = products(masks[:, s, c, :], weights_of(n))
                last.then_inc(group_used, 1)
            for n, (j, k) in enumerate(BATCH_PARTS):
                pe.wait_ge(mask_ready, masks_up_to(CHUNKS - 1) + n)
                products(masks[:, 0, 0, :], weights_of(CHUNKS - 1), stop=True,
                         tiles=range(j, j + k)).then_inc(acc_done, 1)


def kernel(r_x0, L0_rec_W):
    import numpy as np
    import concourse.bacc as bacc
    from concourse.bass_utils import run_bass_kernel_spmd

    xT = np.ascontiguousarray(np.asarray(r_x0).T)
    W = np.ascontiguousarray(np.asarray(L0_rec_W))
    batch = xT.shape[1]

    nc = bacc.Bacc("TRN2", target_bir_lowering=False, num_devices=1)
    xT_dram = nc.dram_tensor("xT_dram", xT.shape, I32, kind="ExternalInput").ap()
    W_dram = nc.dram_tensor("W_dram", W.shape, F32, kind="ExternalInput").ap()
    out_dram = nc.dram_tensor("out_dram", (P, batch // P), F32, kind="ExternalOutput").ap()
    build(nc, xT_dram, W_dram, out_dram)
    r = run_bass_kernel_spmd(nc, [{"xT_dram": xT, "W_dram": W}], core_ids=[0])
    return np.ascontiguousarray(r.results[0]["out_dram"].T).reshape(batch)
```
